# Optimizing a Trainium2 kernel written in Bass

```python
import numpy as np
import jax
import jax.numpy as jnp

def _softmax(x, axis=-1):
    return jax.nn.softmax(x, axis=axis)

def _gelu(x):
    return jax.nn.gelu(x, approximate=True)

def _silu(x):
    return jax.nn.silu(x)

def _sigmoid(x):
    return jax.nn.sigmoid(x)

def _layernorm(x, axis=-1, eps=1e-05):
    m = jnp.mean(x, axis=axis, keepdims=True)
    v = jnp.var(x, axis=axis, keepdims=True)
    return (x - m) / jnp.sqrt(v + eps)

def _scatter_add(tgt, idx, src, axis=0):
    return tgt.at[idx].add(src)

def _segment_sum(src, seg, n):
    return jax.ops.segment_sum(src, seg, n)
kernel_name = 'mk_xattn_seq_d4_seqx_r2_28bf42'

def setup_inputs(seed: int=0):
    np.random.seed(seed)
    _w = jnp.asarray

    def _rec_inputs():
        import jax
        import jax.numpy as jnp
        _rk = jax.random.key(seed)
        x = 7.22e-05 + 1 * jax.random.normal(jax.random.fold_in(_rk, 1), (4, 1024, 512), jnp.float32)
        _lenS = 1024 - jax.random.randint(jax.random.fold_in(_rk, 7), (4,), 0, max(1, 1024 // 4) + 1, jnp.int32)
        _lenS2 = 64 - jax.random.randint(jax.random.fold_in(_rk, 8), (4,), 0, max(1, 64 // 4) + 1, jnp.int32)
        _ctx_2048P = jax.random.normal(jax.random.fold_in(_rk, 11), (4, 16, 1024), jnp.float32)
        _ctx_2048c = jax.random.dirichlet(jax.random.fold_in(_rk, 511), 0.3 * jnp.ones((16,), jnp.float32), (4, 64))
        _ctx_2048t = jnp.einsum('bsk,bkd->bsd', _ctx_2048c, _ctx_2048P)
        _ctx_2048t = _ctx_2048t * jax.lax.rsqrt(jnp.mean(jnp.square(_ctx_2048t)) + 1e-12) * 0.953939
        ctx_2048 = -1.39393e-06 + 0.999914 * (_ctx_2048t + 0.3 * jax.random.normal(jax.random.fold_in(_rk, 611), (4, 64, 1024), jnp.float32))
        _validS = jnp.arange(1024)[None, :] < _lenS[:, None]
        _validS2 = jnp.arange(64)[None, :] < _lenS2[:, None]
        _causal = jnp.tril(jnp.ones((1024, 1024), dtype=bool))
        mask_S_fk1 = jnp.where(_validS[0], 1.0, 0.0).astype(jnp.float32)
        mask_S_fk0 = jnp.where(_validS[0], 0.0, 1.0).astype(jnp.float32)
        return (x, ctx_2048, mask_S_fk1, mask_S_fk0)
    x, ctx_2048, mask_S_fk1, mask_S_fk0 = _rec_inputs()

    def _L0_xattn_setup():
        import jax, jax.numpy as jnp
        import numpy as np
        D_MODEL = 512
        N_HEADS = 16
        N_KV_HEADS = 4
        HEAD_DIM = D_MODEL // N_HEADS
        SPEAKER_DIM = 1024
        EPS = 1e-05

        def rmsnorm(x, w, eps=EPS):
            xf = x.astype(jnp.float32)
            inv = jax.lax.rsqrt(jnp.mean(xf * xf, axis=-1, keepdims=True) + eps)
            return (xf * inv).astype(x.dtype) * w
        key = jax.random.key(seed)
        ks = jax.random.split(key, 7)
        B, T, S = (4, 1024, 256)
        x = jax.random.normal(ks[0], (B, T, D_MODEL), dtype=jnp.float32)
        cond = jax.random.normal(ks[1], (B, S, SPEAKER_DIM), dtype=jnp.float32)
        sq = 0.02
        wq = jax.random.normal(ks[2], (D_MODEL, N_HEADS * HEAD_DIM), dtype=jnp.float32) * sq
        wk = jax.random.normal(ks[3], (SPEAKER_DIM, N_KV_HEADS * HEAD_DIM), dtype=jnp.float32) * sq
        wv = jax.random.normal(ks[4], (SPEAKER_DIM, N_KV_HEADS * HEAD_DIM), dtype=jnp.float32) * sq
        wo = jax.random.normal(ks[5], (N_HEADS * HEAD_DIM, D_MODEL), dtype=jnp.float32) * sq
        norm_w = jnp.ones((D_MODEL,), dtype=jnp.float32)
        return {'x': x, 'cond': cond, 'wq': wq, 'wk': wk, 'wv': wv, 'wo': wo, 'norm_w': norm_w}
    _L0_xattn_all = _L0_xattn_setup()
    _L0_xattn_in = {k: v for k, v in _L0_xattn_all.items() if k in ('wq', 'wk', 'wv', 'wo', 'norm_w')}
    del _L0_xattn_all

    def _L1_xattn_setup():
        import jax, jax.numpy as jnp
        import numpy as np
        HEADS = 16
        HEAD_DIM = 64
        SUPPRESS = 20.0
        key = jax.random.key(seed)
        ks = jax.random.split(key, 8)
        B, HW, C, T, CT = (8, 2048, 512, 77, 1024)
        inner = HEADS * HEAD_DIM
        scale = 0.02
        return {'hidden_states': jax.random.normal(ks[0], (B, HW, C), jnp.float32), 'encoder_hidden_states': jax.random.normal(ks[1], (B, T, CT), jnp.float32), 'mask_A': (jax.random.uniform(ks[2], (HW,)) > 0.5).astype(jnp.float32), 'mask_B': (jax.random.uniform(ks[3], (HW,)) > 0.5).astype(jnp.float32), 'Wq': jax.random.normal(ks[4], (C, inner), jnp.float32) * scale, 'Wk': jax.random.normal(ks[5], (CT, inner), jnp.float32) * scale, 'Wv': jax.random.normal(ks[6], (CT, inner), jnp.float32) * scale, 'Wo': jax.random.normal(ks[7], (inner, C), jnp.float32) * scale, 'bo': jnp.zeros((C,), jnp.float32), 'token_indices_A': jnp.array([2, 3], dtype=jnp.int64), 'token_indices_B': jnp.array([5, 6], dtype=jnp.int64)}
    _L1_xattn_all = _L1_xattn_setup()
    _L1_xattn_in = {k: v for k, v in _L1_xattn_all.items() if k in ('Wq', 'Wk', 'Wv', 'Wo', 'bo', 'token_indices_A', 'token_indices_B')}
    del _L1_xattn_all

    def _L2_xattn_setup():
        import jax, jax.numpy as jnp
        import numpy as np
        D_MODEL = 512
        N_HEADS = 16
        N_KV_HEADS = 4
        HEAD_DIM = D_MODEL // N_HEADS
        SPEAKER_DIM = 1024
        EPS = 1e-05

        def rmsnorm(x, w, eps=EPS):
            xf = x.astype(jnp.float32)
            inv = jax.lax.rsqrt(jnp.mean(xf * xf, axis=-1, keepdims=True) + eps)
            return (xf * inv).astype(x.dtype) * w
        key = jax.random.key(seed)
        ks = jax.random.split(key, 7)
        B, T, S = (4, 1024, 256)
        x = jax.random.normal(ks[0], (B, T, D_MODEL), dtype=jnp.float32)
        cond = jax.random.normal(ks[1], (B, S, SPEAKER_DIM), dtype=jnp.float32)
        sq = 0.02
        wq = jax.random.normal(ks[2], (D_MODEL, N_HEADS * HEAD_DIM), dtype=jnp.float32) * sq
        wk = jax.random.normal(ks[3], (SPEAKER_DIM, N_KV_HEADS * HEAD_DIM), dtype=jnp.float32) * sq
        wv = jax.random.normal(ks[4], (SPEAKER_DIM, N_KV_HEADS * HEAD_DIM), dtype=jnp.float32) * sq
        wo = jax.random.normal(ks[5], (N_HEADS * HEAD_DIM, D_MODEL), dtype=jnp.float32) * sq
        norm_w = jnp.ones((D_MODEL,), dtype=jnp.float32)
        return {'x': x, 'cond': cond, 'wq': wq, 'wk': wk, 'wv': wv, 'wo': wo, 'norm_w': norm_w}
    _L2_xattn_all = _L2_xattn_setup()
    _L2_xattn_in = {k: v for k, v in _L2_xattn_all.items() if k in ('wq', 'wk', 'wv', 'wo', 'norm_w')}
    del _L2_xattn_all

    def _L3_xattn_setup():
        import jax, jax.numpy as jnp
        import numpy as np
        HEADS = 16
        HEAD_DIM = 64
        SUPPRESS = 20.0
        key = jax.random.key(seed)
        ks = jax.random.split(key, 8)
        B, HW, C, T, CT = (8, 2048, 512, 77, 1024)
        inner = HEADS * HEAD_DIM
        scale = 0.02
        return {'hidden_states': jax.random.normal(ks[0], (B, HW, C), jnp.float32), 'encoder_hidden_states': jax.random.normal(ks[1], (B, T, CT), jnp.float32), 'mask_A': (jax.random.uniform(ks[2], (HW,)) > 0.5).astype(jnp.float32), 'mask_B': (jax.random.uniform(ks[3], (HW,)) > 0.5).astype(jnp.float32), 'Wq': jax.random.normal(ks[4], (C, inner), jnp.float32) * scale, 'Wk': jax.random.normal(ks[5], (CT, inner), jnp.float32) * scale, 'Wv': jax.random.normal(ks[6], (CT, inner), jnp.float32) * scale, 'Wo': jax.random.normal(ks[7], (inner, C), jnp.float32) * scale, 'bo': jnp.zeros((C,), jnp.float32), 'token_indices_A': jnp.array([2, 3], dtype=jnp.int64), 'token_indices_B': jnp.array([5, 6], dtype=jnp.int64)}
    _L3_xattn_all = _L3_xattn_setup()
    _L3_xattn_in = {k: v for k, v in _L3_xattn_all.items() if k in ('Wq', 'Wk', 'Wv', 'Wo', 'bo', 'token_indices_A', 'token_indices_B')}
    del _L3_xattn_all
    return {'x': x, 'ctx_2048': ctx_2048, 'mask_S_fk1': mask_S_fk1, 'mask_S_fk0': mask_S_fk0, 'L0_xattn_wq': _L0_xattn_in['wq'], 'L0_xattn_wk': _L0_xattn_in['wk'], 'L0_xattn_wv': _L0_xattn_in['wv'], 'L0_xattn_wo': _L0_xattn_in['wo'], 'L0_xattn_norm_w': _L0_xattn_in['norm_w'], 'L1_xattn_Wq': _L1_xattn_in['Wq'], 'L1_xattn_Wk': _L1_xattn_in['Wk'], 'L1_xattn_Wv': _L1_xattn_in['Wv'], 'L1_xattn_Wo': _L1_xattn_in['Wo'], 'L1_xattn_bo': _L1_xattn_in['bo'], 'L1_xattn_token_indices_A': _L1_xattn_in['token_indices_A'], 'L1_xattn_token_indices_B': _L1_xattn_in['token_indices_B'], 'L2_xattn_wq': _L2_xattn_in['wq'], 'L2_xattn_wk': _L2_xattn_in['wk'], 'L2_xattn_wv': _L2_xattn_in['wv'], 'L2_xattn_wo': _L2_xattn_in['wo'], 'L2_xattn_norm_w': _L2_xattn_in['norm_w'], 'L3_xattn_Wq': _L3_xattn_in['Wq'], 'L3_xattn_Wk': _L3_xattn_in['Wk'], 'L3_xattn_Wv': _L3_xattn_in['Wv'], 'L3_xattn_Wo': _L3_xattn_in['Wo'], 'L3_xattn_bo': _L3_xattn_in['bo'], 'L3_xattn_token_indices_A': _L3_xattn_in['token_indices_A'], 'L3_xattn_token_indices_B': _L3_xattn_in['token_indices_B']}

def reference(x, ctx_2048, mask_S_fk1, mask_S_fk0, L0_xattn_wq, L0_xattn_wk, L0_xattn_wv, L0_xattn_wo, L0_xattn_norm_w, L1_xattn_Wq, L1_xattn_Wk, L1_xattn_Wv, L1_xattn_Wo, L1_xattn_bo, L1_xattn_token_indices_A, L1_xattn_token_indices_B, L2_xattn_wq, L2_xattn_wk, L2_xattn_wv, L2_xattn_wo, L2_xattn_norm_w, L3_xattn_Wq, L3_xattn_Wk, L3_xattn_Wv, L3_xattn_Wo, L3_xattn_bo, L3_xattn_token_indices_A, L3_xattn_token_indices_B):
    import jax
    import jax.numpy as jnp

    def _L0_xattn_ref(x, cond, wq, wk, wv, wo, norm_w):
        import jax, jax.numpy as jnp
        import numpy as np
        D_MODEL = 512
        N_HEADS = 16
        N_KV_HEADS = 4
        HEAD_DIM = D_MODEL // N_HEADS
        SPEAKER_DIM = 1024
        EPS = 1e-05

        def rmsnorm(x, w, eps=EPS):
            xf = x.astype(jnp.float32)
            inv = jax.lax.rsqrt(jnp.mean(xf * xf, axis=-1, keepdims=True) + eps)
            return (xf * inv).astype(x.dtype) * w
        B, T, _ = x.shape
        S = cond.shape[1]
        n_rep = N_HEADS // N_KV_HEADS
        residual = x
        xn = rmsnorm(x, norm_w)
        q = (xn @ wq).reshape(B, T, N_HEADS, HEAD_DIM)
        k = (cond @ wk).reshape(B, S, N_KV_HEADS, HEAD_DIM)
        v = (cond @ wv).reshape(B, S, N_KV_HEADS, HEAD_DIM)
        qg = q.reshape(B, T, N_KV_HEADS, n_rep, HEAD_DIM)
        scale = 1.0 / np.sqrt(HEAD_DIM).astype(np.float32)
        scores = jnp.einsum('btgrd,bsgd->bgrts', qg, k) * scale
        attn = jax.nn.softmax(scores.astype(jnp.float32), axis=-1).astype(q.dtype)
        out = jnp.einsum('bgrts,bsgd->btgrd', attn, v).reshape(B, T, N_HEADS * HEAD_DIM)
        return residual + out @ wo

    def _L1_xattn_ref(hidden_states, encoder_hidden_states, mask_A, mask_B, Wq, Wk, Wv, Wo, bo, token_indices_A, token_indices_B):
        import jax, jax.numpy as jnp
        import numpy as np
        HEADS = 16
        HEAD_DIM = 64
        SUPPRESS = 20.0
        B, HW, C = hidden_states.shape
        T = encoder_hidden_states.shape[1]
        residual = hidden_states
        q = hidden_states @ Wq
        k = encoder_hidden_states @ Wk
        v = encoder_hidden_states @ Wv
        q = q.reshape(B, HW, HEADS, HEAD_DIM).transpose(0, 2, 1, 3)
        k = k.reshape(B, T, HEADS, HEAD_DIM).transpose(0, 2, 1, 3)
        v = v.reshape(B, T, HEADS, HEAD_DIM).transpose(0, 2, 1, 3)
        scale = HEAD_DIM ** (-0.5)
        logits = jnp.einsum('bhqd,bhkd->bhqk', q, k) * scale
        suppress_A_in = 1.0 - mask_A
        suppress_B_in = 1.0 - mask_B
        col_bias = jnp.zeros((HW, T), logits.dtype)
        col_bias = col_bias.at[:, token_indices_A].set((-SUPPRESS * suppress_A_in)[:, None])
        col_bias = col_bias.at[:, token_indices_B].set((-SUPPRESS * suppress_B_in)[:, None])
        logits = logits + col_bias[None, None, :, :]
        probs = jax.nn.softmax(logits, axis=-1)
        out = jnp.einsum('bhqk,bhkd->bhqd', probs, v)
        out = out.transpose(0, 2, 1, 3).reshape(B, HW, HEADS * HEAD_DIM)
        out = out @ Wo + bo
        out = out + residual
        return out

    def _L2_xattn_ref(x, cond, wq, wk, wv, wo, norm_w):
        import jax, jax.numpy as jnp
        import numpy as np
        D_MODEL = 512
        N_HEADS = 16
        N_KV_HEADS = 4
        HEAD_DIM = D_MODEL // N_HEADS
        SPEAKER_DIM = 1024
        EPS = 1e-05

        def rmsnorm(x, w, eps=EPS):
            xf = x.astype(jnp.float32)
            inv = jax.lax.rsqrt(jnp.mean(xf * xf, axis=-1, keepdims=True) + eps)
            return (xf * inv).astype(x.dtype) * w
        B, T, _ = x.shape
        S = cond.shape[1]
        n_rep = N_HEADS // N_KV_HEADS
        residual = x
        xn = rmsnorm(x, norm_w)
        q = (xn @ wq).reshape(B, T, N_HEADS, HEAD_DIM)
        k = (cond @ wk).reshape(B, S, N_KV_HEADS, HEAD_DIM)
        v = (cond @ wv).reshape(B, S, N_KV_HEADS, HEAD_DIM)
        qg = q.reshape(B, T, N_KV_HEADS, n_rep, HEAD_DIM)
        scale = 1.0 / np.sqrt(HEAD_DIM).astype(np.float32)
        scores = jnp.einsum('btgrd,bsgd->bgrts', qg, k) * scale
        attn = jax.nn.softmax(scores.astype(jnp.float32), axis=-1).astype(q.dtype)
        out = jnp.einsum('bgrts,bsgd->btgrd', attn, v).reshape(B, T, N_HEADS * HEAD_DIM)
        return residual + out @ wo

    def _L3_xattn_ref(hidden_states, encoder_hidden_states, mask_A, mask_B, Wq, Wk, Wv, Wo, bo, token_indices_A, token_indices_B):
        import jax, jax.numpy as jnp
        import numpy as np
        HEADS = 16
        HEAD_DIM = 64
        SUPPRESS = 20.0
        B, HW, C = hidden_states.shape
        T = encoder_hidden_states.shape[1]
        residual = hidden_states
        q = hidden_states @ Wq
        k = encoder_hidden_states @ Wk
        v = encoder_hidden_states @ Wv
        q = q.reshape(B, HW, HEADS, HEAD_DIM).transpose(0, 2, 1, 3)
        k = k.reshape(B, T, HEADS, HEAD_DIM).transpose(0, 2, 1, 3)
        v = v.reshape(B, T, HEADS, HEAD_DIM).transpose(0, 2, 1, 3)
        scale = HEAD_DIM ** (-0.5)
        logits = jnp.einsum('bhqd,bhkd->bhqk', q, k) * scale
        suppress_A_in = 1.0 - mask_A
        suppress_B_in = 1.0 - mask_B
        col_bias = jnp.zeros((HW, T), logits.dtype)
        col_bias = col_bias.at[:, token_indices_A].set((-SUPPRESS * suppress_A_in)[:, None])
        col_bias = col_bias.at[:, token_indices_B].set((-SUPPRESS * suppress_B_in)[:, None])
        logits = logits + col_bias[None, None, :, :]
        probs = jax.nn.softmax(logits, axis=-1)
        out = jnp.einsum('bhqk,bhkd->bhqd', probs, v)
        out = out.transpose(0, 2, 1, 3).reshape(B, HW, HEADS * HEAD_DIM)
        out = out @ Wo + bo
        out = out + residual
        return out
    x = _L0_xattn_ref(x, ctx_2048, L0_xattn_wq, L0_xattn_wk, L0_xattn_wv, L0_xattn_wo, L0_xattn_norm_w)
    x = _L1_xattn_ref(x, ctx_2048, mask_S_fk1, mask_S_fk0, L1_xattn_Wq, L1_xattn_Wk, L1_xattn_Wv, L1_xattn_Wo, L1_xattn_bo, L1_xattn_token_indices_A, L1_xattn_token_indices_B)
    x = _L2_xattn_ref(x, ctx_2048, L2_xattn_wq, L2_xattn_wk, L2_xattn_wv, L2_xattn_wo, L2_xattn_norm_w)
    x = _L3_xattn_ref(x, ctx_2048, mask_S_fk1, mask_S_fk0, L3_xattn_Wq, L3_xattn_Wk, L3_xattn_Wv, L3_xattn_Wo, L3_xattn_bo, L3_xattn_token_indices_A, L3_xattn_token_indices_B)
    return x

_drawn_inputs = setup_inputs


def setup_inputs(seed=0):
    import zlib

    import numpy as np

    out = dict(_drawn_inputs(seed))
    spreads = {'L0_xattn_norm_w': (1.0, 0.6),
     'L1_xattn_bo': (0.0, 0.1),
     'L2_xattn_norm_w': (1.0, 0.6),
     'L3_xattn_bo': (0.0, 0.1)}
    factors = {'mask_S_fk1': 8.0,
     'mask_S_fk0': 8.0,
     'L0_xattn_wq': 3.728,
     'L0_xattn_wk': 3.677,
     'L1_xattn_Wq': 2.688,
     'L1_xattn_Wk': 2.673,
     'L2_xattn_wq': 3.715,
     'L2_xattn_wk': 3.655}
    for name, (base, spread) in spreads.items():
        noise = np.random.default_rng([zlib.crc32(name.encode()), seed]).standard_normal(out[name].shape)
        drawn = base * np.exp(spread * noise) if base else spread * noise
        out[name] = jnp.asarray(drawn.astype(out[name].dtype))
    for name, factor in factors.items():
        out[name] = (out[name] * factor).astype(out[name].dtype)
    return out
```

```python
from contextlib import ExitStack

import numpy as np

import concourse.bass as bass
from concourse import mybir

F32 = mybir.dt.float32
F32R = mybir.dt.float32r
I32 = mybir.dt.int32
ALU = mybir.AluOpType
ACT = mybir.ActivationFunctionType
AX_X = mybir.AxisListType.X

P = 128
BATCH = 4
TOKENS = 1024
D = 512
DC = D // P
KEYS = 64
CTX = 1024
CC = CTX // P
HEADS = 16
KVH = 4
HD_G = D // HEADS
HK = HEADS * KEYS
KC = HK // P
BLK = 512
NBLK = TOKENS // BLK
TT = BLK // P
HALF = 512
HH = HALF // KEYS
STEPS = 8
PAIRS = 2
ITS = PAIRS * BATCH
G_SCALE = float(np.float32(1.0) / np.sqrt(np.float32(HD_G)))
M_SCALE = 0.125
SUPPRESS = 20.0
EPS = 1e-5
AUX = TT * NBLK * KEYS + DC


def bass_cross_attention_stack(nc, xT, ctxT, wkvM, wkvG, wqG, woG, wqM, woM, normw, bo, masks, idx, xs):
    ctx = ExitStack()
    with ctx:
        def sb(name, shape, dt=F32):
            return ctx.enter_context(nc.sbuf_tensor(name, shape, dt))

        def sem(name):
            return ctx.enter_context(nc.semaphore(name))

        sKVM = nc.dram_tensor("s_kvm", (8, BATCH, P, 4 * P), F32, kind="Internal").ap()
        sKVMh = sKVM.rearrange("(a h) b p n -> a h b p n", h=2)
        sKG = nc.dram_tensor("s_kg", (PAIRS, BATCH, P, 2, HK), F32, kind="Internal").ap()
        sVG = nc.dram_tensor("s_vg", (PAIRS, BATCH, P, 2, HK), F32, kind="Internal").ap()
        sWG = nc.dram_tensor("s_wg", (PAIRS, 2, P, 2, DC * D), F32, kind="Internal").ap()
        sAux = nc.dram_tensor("s_aux", (PAIRS, P, AUX), F32, kind="Internal").ap()

        foldM = sb("foldM", [P, 2, DC, HK], F32R)
        foldN = sb("foldN", [P, 2, KC, D], F32R)
        qT = foldM[:, :, 0:2, :].rearrange("p s a (b n) -> p s (a b) n", n=BLK)
        kG = foldM[:, :, 2, :]
        oT = foldN[:, :, 0:2, :]
        X = [sb(f"x{b}", [P, DC, BLK]) for b in range(NBLK)]
        xhl = sb("xhl", [P, 2, DC, BLK], F32R)
        xqhl = sb("xqhl", [P, 2, 2, BLK], F32R)
        xsq = sb("xsq", [P, 2, BLK])
        sqsum = sb("sqsum", [P, BLK])
        prob = [sb(f"prob{b}", [P, TT, HK]) for b in range(2)]
        pT = sb("pT", [P, 2, 2, BLK], F32R)
        vG = sb("vG", [P, 2, KC, P], F32R)
        wq = sb("wq", [P, 2, DC, D], F32R)
        wo = sb("wo", [P, 2, DC, D], F32R)
        ring = sb("ring", [P, 4, BLK])
        kv = sb("kv", [P, 2, 4 * P])
        aux = sb("aux", [P, AUX])
        ident = sb("ident", [P, P])
        small = sb("small", [P, 64])
        tiny = sb("tiny", [P, 8])
        inv = [small[:, 4:8], small[:, 8:12]]
        mhalf = small[:, 12:16]
        hmax = [small[:, 16:24], small[:, 56:64]]
        hsum = [small[:, 24:32], tiny[:, 0:8]]
        rsum = [small[:, 32:40], small[:, 40:48]]
        gscale = small[:, 49:53]
        ones = small[:, 48:49]
        bias = aux[:, 0:TT * NBLK * KEYS].rearrange("p (t k) -> p t k", k=KEYS)
        bout = aux[:, TT * NBLK * KEYS:AUX]

        def bank(name):
            return ctx.enter_context(nc.psum_tensor(name, [P, 512], F32))

        OB = [bank(f"OB{c}") for c in range(4)]
        TB = bank("TB")
        MX = bank("MX")
        SB = [bank(f"SB{i}") for i in range(2)]
        PB = [TB, MX, SB[0], SB[1]]

        names = ("ctx_in repeated kvp kv_evac g_done g_hi g_stage wsp_in wsp_scaled wsp_hi wsp c_in "
                 "c_made c_f c_eq c_m1 c_m2 c_sel c_scale bias_a aux_ok aux_st zero idented ld_wq ld_vg "
                 "ld_wo ld_kg ld_x0 ld_x1 ld_aux ld_kv stored0 stored1 scores copied biased maxed evac "
                 "exped hsummed summed normed trans pt_hi pt_lo mixed ot_hi ot_lo outd xnew xb_hi xb_lo "
                 "qchunk qd q_hi q_lo x_hi x_lo x_sq rmsd sq_added powd invd fold fold_hi fold_lo").split()
        S = {n: sem("s_" + n) for n in names}
        w0_in = [sem(f"s_w0_in{i}") for i in range(2)]
        wg_in = [sem(f"s_wg_in{i}") for i in range(2)]
        kv_st = [sem(f"s_kv_st{i}") for i in range(4)]
        g_st = [sem(f"s_g_st{i}") for i in range(4)]
        wsp_st = [sem(f"s_wsp_st{i}") for i in range(2)]
        ld_ring = [sem(f"s_ld_ring{i}") for i in range(4)]

        block = ctx.enter_context(nc.Block())

        cx = prob[0][:, 0:2, :].rearrange("p a (b n) -> p (a b) n", n=BATCH * KEYS)
        w0 = prob[0][:, 2:4, :].rearrange("p a n -> p (a n)").rearrange("p (s c m) -> p s c m", s=2, c=CC)
        stM = prob[1][:, 0:2, :].rearrange("p a (s b m) -> p (a s) b m", s=2, b=BATCH)
        rep = prob[1][:, 2:4, :].rearrange("p a n -> p (a n)").rearrange("p (s c m) -> p s c m", s=2, c=CC)
        wG = X[0][:, :, :].rearrange("p a n -> p (a n)").rearrange("p (s c m) -> p s c m", s=2, c=CC)
        flatM = foldM[:, :, :, :].rearrange("p s c n -> p (s c n)")
        stK = [flatM[:, i * 2048:(i + 1) * 2048].rearrange("p (s b n) -> p s b n", s=2, b=BATCH) for i in range(2)]
        stV = [flatM[:, i * 2048:(i + 1) * 2048].rearrange("p (s t n) -> p s t n", s=2, t=KC) for i in range(2, 4)]
        stW = [foldN[:, :, 4 * i:4 * i + 4, :] for i in range(2)]

        def diagonals(n, bank, part):
            if n < 4:
                return [(stK[n % 2][32 * r:32 * r + 32, part, :, KEYS * r:KEYS * (r + 1)],
                         bank[32 * r:32 * r + 32, 0:BATCH * KEYS].rearrange("p (b k) -> p b k", k=KEYS))
                        for r in range(4)]
            pieces = []
            for a in range(2):
                for odd in range(2):
                    rows, col = slice(64 * a, 64 * a + 64), HD_G * (2 * odd + a)
                    pieces.append((stV[n % 2][rows, part, odd::2, col:col + HD_G],
                                   bank[rows, 0:P].rearrange("p (g d) -> p g d", d=HD_G)))
            return pieces

        def fold_part(ph, t, part):
            if ph == 2:
                return (PB[t % 4][:, :].rearrange("p (c m) -> p c m", c=DC), foldM[:, part, :, t * P:(t + 1) * P])
            return PB[t % 4][:, :], foldN[:, part, t, :]

        @block.sync
        def _(sp):
            sp.dma_start(cx, ctxT).then_inc(S["ctx_in"], 16)
            for j in range(2):
                sp.dma_start(w0[:, j], wkvM[j]).then_inc(w0_in[j], 16)
            sp.dma_start(small[:, 56:60].bitcast(I32), idx[0].partition_broadcast(P)).then_inc(S["c_in"], 16)
            sp.dma_start(small[:, 60:64].bitcast(I32), idx[1].partition_broadcast(P)).then_inc(S["c_in"], 16)
            sp.dma_start(xsq[:, 0, 0:16], masks).then_inc(S["c_in"], 16)
            sp.dma_start(xsq[:, 0, 16:24], normw).then_inc(S["c_in"], 16)
            sp.dma_start(xsq[:, 0, 24:32], bo).then_inc(S["c_in"], 16)

            def kv_weights(n, j):
                sp.wait_ge(S["kvp"], n - 1)
                sp.dma_start(w0[:, j % 2], wkvM[n]).then_inc(w0_in[j % 2], 16)
            kv_weights(2, 0)
            kv_weights(3, 3)
            for n in range(2):
                sp.dma_start(wG[:, n], wkvG[0, n]).then_inc(wg_in[n], 16)
            with sp.Fori(1, 8) as g:
                for j in range(4):
                    kv_weights(4 * g + j, j)
            sp.dma_start(xs[0:BATCH, 0], xT[:, 0]).then_inc(S["stored0"], 16)
            sp.dma_start(xs[0:BATCH, 1], xT[:, 1]).then_inc(S["stored1"], 16)
            for n in range(2):
                sp.wait_ge(S["g_done"], 4 * (n + 1))
                sp.dma_start(wG[:, n], wkvG[1, n]).then_inc(wg_in[n], 16)

            def body(it, first):
                if first:
                    lp, b, it2 = 0, 0, 0
                    value = lambda factor, plus=0: factor * it + plus
                else:
                    known = {}

                    def value(factor, plus=0):
                        if (factor, plus) not in known:
                            known[factor, plus] = sp.snap(factor * it + plus)
                        return known[factor, plus]
                    lp, b = sp.snap(it // BATCH), (it - BATCH * (it // BATCH)).with_bounds(min_val=0, max_val=BATCH - 1)
                    for factor, plus in ([(16, 16), (32, -23), (16, 0), (16, -8), (32, 0)] + [(16, n - 3) for n in range(4)]
                                         + [(8, n) for n in range(1, 9)] + [(16, n) for n in range(1, 13)]):
                        value(factor, plus)
                if first:
                    for i in range(2):
                        sp.wait_ge(wsp_st[i], 2 * 16)
                    sp.wait_ge(S["aux_st"], 2 * 16)
                    sp.wait_ge(S["stored0"], 16)
                    sp.wait_ge(S["stored1"], 16)
                else:
                    sp.wait_ge(S["stored0"], value(16))
                    sp.wait_ge(S["stored1"], value(16))
                    sp.wait_ge(S["scores"], value(32, -23))
                sp.dma_start(wq[:, :, :, :].bitcast(F32).rearrange("p s c n -> p s (c n)"), sWG[lp, 0]
                             ).then_inc(S["ld_wq"], 16)

                def ring_load(n, src):
                    if n < 4:
                        if not first:
                            sp.wait_ge(S["fold"], value(16, n - 3))
                    elif n < 12:
                        sp.wait_ge(S["x_lo"], value(8, n - 3))
                        sp.wait_ge(S["x_sq"], value(8, n - 3))
                    else:
                        sp.wait_ge(S["fold"], value(16, n - 11))
                    sp.dma_start(ring[:, n % 4], src).then_inc(ld_ring[n % 4], 16)

                for c in range(DC):
                    ring_load(c, xs[it, 0, :, c, :])
                if first:
                    for i in range(4):
                        sp.wait_ge(g_st[i], 4 * 16)
                else:
                    sp.wait_ge(S["outd"], value(16, -8))
                sp.dma_start(vG[:, :, :, :].bitcast(F32).rearrange("p s t m -> p s (t m)"), sVG.rearrange("l b p s n -> (l b) p s n")[it]
                             ).then_inc(S["ld_vg"], 16)
                sp.dma_start(wo[:, :, :, :].bitcast(F32).rearrange("p s c n -> p s (c n)"), sWG[lp, 1]
                             ).then_inc(S["ld_wo"], 16)
                if not first:
                    sp.wait_ge(S["scores"], value(32))
                sp.dma_start(kG.bitcast(F32), sKG.rearrange("l b p s n -> (l b) p s n")[it]).then_inc(S["ld_kg"], 16)
                for c in range(DC):
                    ring_load(4 + c, xs[it, 1, :, c, :])
                if first:
                    sp.wait_ge(S["g_done"], 8 * PAIRS)
                else:
                    sp.wait_ge(S["stored0"], value(16, 16))
                sp.dma_start(X[0][:, :, :], xs[it, 0]).then_inc(S["ld_x0"], 16)
                if first:
                    for i in range(4):
                        sp.wait_ge(kv_st[i], 8 * 16)
                else:
                    sp.wait_ge(S["fold"], value(16))
                sp.dma_start(kv[:, :, :], sKVMh[lp * 2, :, b].rearrange("h p n -> p h n")).then_inc(S["ld_kv"], 16)
                for t in range(4):
                    ring_load(8 + t, wqM[lp, t])
                if not first:
                    sp.wait_ge(S["xnew"], value(16))
                sp.dma_start(aux[:, :], sAux[lp]).then_inc(S["ld_aux"], 16)
                if not first:
                    sp.wait_ge(S["stored1"], value(16, 16))
                sp.dma_start(X[1][:, :, :], xs[it, 1]).then_inc(S["ld_x1"], 16)
                for t in range(4, KC):
                    ring_load(8 + t, wqM[lp, t])
                sp.wait_ge(S["fold"], value(16, 8))
                sp.dma_start(kv[:, :, :], sKVMh[lp * 2 + 1, :, b].rearrange("h p n -> p h n")).then_inc(S["ld_kv"], 16)
                for t in range(KC):
                    ring_load(16 + t, woM[lp, t])

            body(0, True)
            with sp.Fori(1, ITS) as it:
                body(it, False)
            sp.wait_ge(S["stored0"], 16 * (ITS + 1))
            sp.wait_ge(S["stored1"], 16 * (ITS + 1))

        @block.tensor
        def _(pe):
            def three(out, a_hi, a_lo, b_hi, b_lo, start, stop):
                pe.matmul(out, a_hi, b_hi, start=start, stop=False)
                pe.matmul(out, a_hi, b_lo, start=False, stop=False)
                return pe.matmul(out, a_lo, b_hi, start=False, stop=stop)

            pe.wait_ge(S["ctx_in"], 16)

            def kv_job(half, j):
                pe.wait_ge(w0_in[j % 2], 16 * (half + 1))
                for c in range(CC):
                    last = pe.matmul(OB[j][:, 0:BATCH * KEYS], w0[:, j % 2, c, :], cx[:, c, :],
                                     start=(c == 0), stop=(c == CC - 1))
                last.then_inc(S["kvp"], 1)
            for j in range(4):
                kv_job(j // 2, j)
            with pe.Fori(1, 8) as g:
                for j in range(4):
                    pe.wait_ge(S["kv_evac"], 4 * g + j - 3)
                    kv_job(2 * g + j // 2, j)
            for lp in range(PAIRS):
                for n in range(8):
                    i = 8 * lp + n
                    pe.wait_ge(S["repeated"], i + 1)
                    if n == 4:
                        pe.wait_ge(wg_in[1], 16 * (lp + 1))
                    if i >= 4:
                        pe.wait_ge(S["g_stage"], i - 3)
                    else:
                        pe.wait_ge(S["kv_evac"], 32)
                    for c in range(CC):
                        lhsT = rep[:, i % 2, c, :]
                        rhs = cx[:, c, :] if n < 4 else wG[:, 1, c, :]
                        out = OB[i % 4][:, 0:BATCH * KEYS if n < 4 else P]
                        last = pe.matmul(out, lhsT, rhs, start=(c == 0), stop=(c == CC - 1))
                    last.then_inc(S["g_done"], 1)
            pe.wait_ge(S["idented"], 4)
            pe.wait_ge(S["g_stage"], 16)

            def q_bound(it, ph, first):
                k = 4 * it + ph
                a = 2 * it + ph
                pe.wait_ge(S["ld_wq"], 16 * (it + 1))
                for c in range(DC):
                    pe.wait_ge(S["x_lo"], 4 * a + c + 1)
                    for j in range(4):
                        if c == 0 and not (first and ph == 0):
                            if j == 0 and not (first and ph == 1):
                                pe.wait_ge(S["pt_lo"], 8 * (k - 1))
                            elif j == 0:
                                pe.wait_ge(S["q_lo"], 1)
                            elif j == 1 and ph == 0:
                                pe.wait_ge(S["fold_lo"], 16 * it)
                            elif j == 1:
                                pe.wait_ge(S["q_lo"], 4 * a)
                            else:
                                pe.wait_ge(S["evac"], 8 * k + j - 3)
                        last = three(PB[j][:, :], wq[:, 0, c, j * P:(j + 1) * P], wq[:, 1, c, j * P:(j + 1) * P],
                                     xqhl[:, 0, c % 2, :], xqhl[:, 1, c % 2, :], c == 0, c == DC - 1)
                        if c == DC - 1:
                            last.then_inc(S["qd"], 1)
                    if c < DC - 1:
                        last.then_inc(S["qchunk"], 1)
                pe.wait_ge(S["sq_added"], 3 * a + 3)
                if not first:
                    pe.wait_ge(S["xnew"], 4 * (k - 1))
                elif ph == 1:
                    pe.wait_ge(S["rmsd"], 1)
                for tt in range(TT):
                    last = pe.matmul(OB[3][:, tt:tt + 1], sqsum[:, tt * P:(tt + 1) * P], ones, start=True, stop=True)
                last.then_inc(S["qchunk"], 1)

            def fold_bound(it, ph):
                k = 4 * it + ph
                pe.wait_ge(S["ld_kv"], 16 * (2 * it + ph - 1))
                for t in range(KC):
                    i = 8 * (ph - 2) + t
                    pe.wait_ge(ld_ring[t % 4], 16 * (6 * it + 2 + i // 4 + 1))
                    if t >= 4:
                        pe.wait_ge(S["fold_lo"], 16 * it + i - 3)
                    elif t == 0:
                        pe.wait_ge(S["pt_lo"], 8 * (k - 1))
                    elif t == 1:
                        pe.wait_ge(S["ot_lo"], 4 * (2 * it + ph - 1))
                    else:
                        pe.wait_ge(S["evac"], 8 * k + t - 3)
                    blk = kv[:, t // 4, (t % 4) * P:(t % 4 + 1) * P]
                    if ph == 2:
                        for c in range(DC):
                            last = pe.matmul(PB[t % 4][:, c * P:(c + 1) * P], ring[:, t % 4, c * P:(c + 1) * P], blk,
                                             start=True, stop=True)
                    else:
                        last = pe.matmul(PB[t % 4][:, :], blk, ring[:, t % 4, :], start=True, stop=True)
                    last.then_inc(S["fold"], 1)

            def transposes(it, ph, t, tail=False):
                k = 4 * it + ph
                pr = prob[(ph - 1) % 2]
                pe.wait_ge(S["normed"], 8 * (k - 1) + 4 * (t // 4) + 4)
                if t > 0 or tail:
                    pe.wait_ge(S["pt_lo"], 8 * (k - 1) + t)
                elif ph < 2:
                    pe.wait_ge(S["q_lo"], 4 * (2 * it + ph) + 1)
                else:
                    pe.wait_ge(S["fold_lo"], 16 * it + 8 * (ph - 2) + 5)
                for tt in range(TT):
                    last = pe.transpose(TB[:, tt * P:(tt + 1) * P], pr[:, tt, t * P:(t + 1) * P], ident[:, :])
                last.then_inc(S["trans"], 1)

            def open_out(it, ph, c, first, tail=False):
                k = 4 * it + ph
                if not (first and ph == 1):
                    pe.wait_ge(S["xnew"], 4 * (k - 2) + c + 1)
                if c == 3 and ph < 2 and not tail:
                    pe.wait_ge(S["rmsd"], 2 * it + ph + 1)

            def product(it, ph, t, first, tail=False):
                k = 4 * it + ph
                pe.wait_ge(S["pt_lo"], 8 * (k - 1) + t + 1)
                if ph in (0, 3):
                    if ph == 3:
                        pe.wait_ge(S["fold_lo"], 16 * it + 8 + t + 1)
                    for c in range(DC):
                        if t == 0:
                            open_out(it, ph, c, first, tail)
                        last = three(OB[c][:, :], foldN[:, 0, t, c * P:(c + 1) * P], foldN[:, 1, t, c * P:(c + 1) * P],
                                     pT[:, t % 2, 0, :], pT[:, t % 2, 1, :], t == 0, t == KC - 1)
                        if t == KC - 1:
                            last.then_inc(S["outd"], 1)
                    return
                a = 2 * it + ph - 1
                if t == 0:
                    pe.wait_ge(S["ld_vg"], 16 * (it + 1))
                if t % 2 == 0:
                    if t > 0:
                        pe.wait_ge(S["ot_lo"], 4 * a + t // 2)
                    elif ph == 1:
                        pe.wait_ge(S["q_lo"], 4 * (a + 1) + 2)
                    else:
                        pe.wait_ge(S["fold_lo"], 16 * it + 6)
                last = three(MX[:, :], vG[:, 0, t, :], vG[:, 1, t, :], pT[:, t % 2, 0, :], pT[:, t % 2, 1, :],
                             t % 2 == 0, t % 2 == 1)
                if t % 2 == 1:
                    last.then_inc(S["mixed"], 1)

            def out_part(it, ph, j, part, first):
                a = 2 * it + ph - 1
                pe.wait_ge(S["ot_lo"], 4 * a + j + 1)
                if j == 0:
                    pe.wait_ge(S["ld_wo"], 16 * (it + 1))
                for c in (2 * part, 2 * part + 1):
                    if j == 0:
                        open_out(it, ph, c, first)
                    last = three(OB[c][:, :], wo[:, 0, j, c * P:(c + 1) * P], wo[:, 1, j, c * P:(c + 1) * P],
                                 oT[:, 0, j % 2, :], oT[:, 1, j % 2, :], j == 0, j == 3)
                    if j == 3:
                        last.then_inc(S["outd"], 1)

            def scores(it, ph, u):
                k = 4 * it + ph
                hf, tt = u // 4, u % 4
                if u >= 2 and ph < 2:
                    pe.wait_ge(S["copied"], 16 * it + 8 * ph + u - 1)
                elif u >= 2:
                    pe.wait_ge(S["biased"], 16 * it + 8 * (ph - 2) + u - 1)
                out = SB[u % 2]
                tok = slice(tt * P, (tt + 1) * P)
                if ph < 2:
                    a = 2 * it + ph
                    if u == 0:
                        pe.wait_ge(S["q_lo"], 4 * a + 3)
                        pe.wait_ge(S["ld_kg"], 16 * (it + 1))
                    if u == 1:
                        pe.wait_ge(S["q_lo"], 4 * a + 4)
                    for i in range(2):
                        j = 2 * hf + i
                        last = three(out[:, i * 256:(i + 1) * 256], qT[:, 0, j, tok], qT[:, 1, j, tok],
                                     kG[:, 0, j * 256:(j + 1) * 256], kG[:, 1, j * 256:(j + 1) * 256], True, True)
                else:
                    if u == 0:
                        pe.wait_ge(S["fold_lo"], 16 * it + 8 * (ph - 2) + 7)
                    if u == 1:
                        pe.wait_ge(S["fold_lo"], 16 * it + 8 * (ph - 2) + 8)
                    for c in range(DC):
                        if u == 0:
                            pe.wait_ge(S["xb_hi"], 4 * (2 * it + ph - 2) + c + 1)
                            pe.wait_ge(S["xb_lo"], 4 * (2 * it + ph - 2) + c + 1)
                        last = three(out[:, :], xhl[:, 0, c, tok], xhl[:, 1, c, tok],
                                     foldM[:, 0, c, hf * HALF:(hf + 1) * HALF], foldM[:, 1, c, hf * HALF:(hf + 1) * HALF],
                                     c == 0, c == DC - 1)
                last.then_inc(S["scores"], 1)

            def phase(it, ph, first, tail=False):
                out_of = not (first and ph == 0)
                grouped = ph in (1, 2)
                for u in range(STEPS):
                    if out_of:
                        transposes(it, ph, u, tail)
                        if u > 0:
                            product(it, ph, u - 1, first, tail)
                        if grouped and u >= 3:
                            out_part(it, ph, (u - 3) // 2, (u - 3) % 2, first)
                        if grouped and u == STEPS - 1:
                            product(it, ph, KC - 1, first, tail)
                    if not tail:
                        scores(it, ph, u)
                if out_of:
                    if not grouped:
                        product(it, ph, KC - 1, first, tail)
                    else:
                        out_part(it, ph, 2, 1, first)
                        out_part(it, ph, 3, 0, first)
                        out_part(it, ph, 3, 1, first)

            def body(it, first):
                for ph in range(4):
                    if ph < 2:
                        q_bound(it, ph, first)
                    else:
                        fold_bound(it, ph)
                    phase(it, ph, first)

            body(0, True)
            with pe.Fori(1, ITS) as it:
                body(it, False)
            phase(ITS, 0, False, tail=True)

        @block.scalar
        def _(act):
            for lp in range(PAIRS):
                act.wait_ge(S["aux_ok"], lp + 1)
                act.wait_ge(S["bias_a"], 16 * (lp + 1))
                act.dma_start(sAux[lp], aux[:, :]).then_inc(S["aux_st"], 16)
            def kv_store(g, j):
                act.wait_ge(S["kv_evac"], 4 * g + j + 1)
                act.dma_start(sKVM[g].rearrange("b p n -> p b n")[:, :, j * P:(j + 1) * P], stM[:, j]
                              ).then_inc(kv_st[j], 16)
            for j in range(4):
                kv_store(0, j)
            with act.Fori(1, 8) as g:
                for j in range(4):
                    kv_store(g, j)
            act.wait_ge(S["zero"], 2)
            for lp in range(PAIRS):
                for n in range(8):
                    i = 8 * lp + n
                    act.wait_ge(S["g_done"], i + 1)
                    s = n % 2 + 2 * (n // 4)
                    if i >= 8 or n % 4 >= 2:
                        act.wait_ge(g_st[s], 16 * (2 * lp + (n % 4) // 2))
                    for dst, src in diagonals(n, OB[i % 4], 0):
                        last = act.activation(dst, src, ACT.Copy)
                    last.then_inc(S["g_hi"], 1)
                    act.wait_ge(S["g_stage"], i + 1)
                    if n < 4:
                        act.dma_start(sKG[lp].rearrange("b p s n -> p s b n")[:, :, :, n * 256:(n + 1) * 256],
                                      stK[n % 2].bitcast(F32)).then_inc(g_st[s], 16)
                    else:
                        act.dma_start(sVG[lp, n - 4], stV[n % 2].bitcast(F32).rearrange("p s t m -> p s (t m)")
                                      ).then_inc(g_st[s], 16)

            def body(it, first):
                for ph in range(4):
                    k = 4 * it + ph
                    if ph < 2:
                        a = 2 * it + ph
                        if ph == 0:
                            x_hi(it, 0, 0, first)
                            x_hi(it, 0, 1, first)
                            if not first:
                                exp(it - 1, 3, STEPS - 1)
                        for c in range(2, DC):
                            x_hi(it, ph, c, first)
                        if first and ph == 0:
                            for i in range(4):
                                act.wait_ge(g_st[i], 4 * 16)
                                act.wait_ge(kv_st[i], 8 * 16)
                        for j in range(4):
                            act.wait_ge(S["qd"], 4 * a + j + 1)
                            act.activation(qT[:, 0, j, :], PB[j][:, :], ACT.Copy).then_inc(S["q_hi"], 1)
                    else:
                        for t in range(KC):
                            act.wait_ge(S["fold"], 16 * it + 8 * (ph - 2) + t + 1)
                            src, dst = fold_part(ph, t, 0)
                            act.activation(dst, src, ACT.Copy).then_inc(S["fold_hi"], 1)
                    out_of = not (first and ph == 0)
                    grouped = ph in (1, 2)
                    for u in range(STEPS):
                        if out_of:
                            pt_hi(k, u)
                        if grouped and u >= 2 and u % 2 == 0:
                            ot_hi(2 * it + ph - 1, u // 2 - 1)
                        if u == 1 and ph == 0 and not first:
                            store(it - 1, 0)
                        if u == 1 and ph == 1 and not first:
                            store(it - 1, 1)
                        if ph == 0 and u == 6:
                            x_hi(it, 1, 0, first)
                            x_hi(it, 1, 1, first)
                        if grouped and u == STEPS - 1:
                            ot_hi(2 * it + ph - 1, 3)
                        if ph < 2:
                            act.wait_ge(S["scores"], 8 * k + u + 1)
                            act.activation(prob[ph][:, u % 4, (u // 4) * HALF:(u // 4 + 1) * HALF], SB[u % 2][:, :],
                                           ACT.Copy).then_inc(S["copied"], 1)
                            if u > 0:
                                exp(it, ph, u - 1)
                            if u == STEPS - 1:
                                exp(it, ph, u)
                        elif ph < 3 or u < STEPS - 1:
                            exp(it, ph, u)
                    if grouped:
                        for c in range(DC):
                            act.wait_ge(S["xnew"], 4 * (k - 1) + c + 1)
                            act.activation(xhl[:, 0, c, :], X[ph - 1][:, c, :], ACT.Copy).then_inc(S["xb_hi"], 1)

            def exp(it, ph, u):
                k = 4 * it + ph
                act.wait_ge(S["evac"], 8 * k + u + 1)
                own = prob[ph % 2][:, u % 4, (u // 4) * HALF:(u // 4 + 1) * HALF]
                if ph < 2:
                    if u == 0:
                        act.wait_ge(S["invd"], 2 * it + ph + 1)
                    act.activation(own, own, ACT.Exp, scale=inv[ph][:, u % 4:u % 4 + 1]).then_inc(S["exped"], 1)
                else:
                    act.activation(own, own, ACT.Exp).then_inc(S["exped"], 1)

            def x_hi(it, ph, c, first):
                a = 2 * it + ph
                act.wait_ge(ld_ring[c], 16 * (6 * it + ph + 1))
                if not (first and ph == 0 and c < 2):
                    act.wait_ge(S["qchunk"], 4 * a + c - 1)
                act.activation(xqhl[:, 0, c % 2, :], ring[:, c, :], ACT.Copy).then_inc(S["x_hi"], 1)
                if c >= 2:
                    act.wait_ge(S["sq_added"], 3 * a + 1)
                elif not (first and ph == 0):
                    act.wait_ge(S["sq_added"], 3 * a - 1 + c)
                act.activation(xsq[:, c % 2, :], ring[:, c, :], ACT.Square).then_inc(S["x_sq"], 1)

            def pt_hi(k, t):
                act.wait_ge(S["trans"], 8 * (k - 1) + t + 1)
                act.activation(pT[:, t % 2, 0, :], TB[:, :], ACT.Copy).then_inc(S["pt_hi"], 1)

            def ot_hi(a, j):
                act.wait_ge(S["mixed"], 4 * a + j + 1)
                act.activation(oT[:, 0, j % 2, :], MX[:, :], ACT.Copy).then_inc(S["ot_hi"], 1)

            def store(it, blk):
                act.wait_ge(S["xnew"], 16 * it + 4 * (3 + blk))
                act.dma_start(xs[it + BATCH, blk], X[blk][:, :, :]).then_inc(S[f"stored{blk}"], 16)

            body(0, True)
            with act.Fori(1, ITS) as it:
                body(it, False)
            exp(ITS - 1, 3, STEPS - 1)
            store(ITS - 1, 0)
            for t in range(KC):
                pt_hi(4 * ITS, t)
            store(ITS - 1, 1)

        @block.vector
        def _(dve):
            def lo_part(out, psum, hi):
                return dve.tensor_tensor(out, psum, hi.bitcast(F32), ALU.subtract)

            dve.memset(stM, 0.0).then_inc(S["zero"], 1)
            dve.memset(flatM.bitcast(F32), 0.0).then_inc(S["zero"], 1)
            dve.memset(small[:, 12:16], -0.5).then_inc(S["idented"], 1)
            dve.memset(gscale, G_SCALE).then_inc(S["idented"], 1)
            dve.memset(ones, 1.0).then_inc(S["idented"], 1)

            dve.wait_ge(S["c_in"], 5 * 16)
            dve.tensor_copy(xsq[:, 1, 0:8], small[:, 56:64].bitcast(I32)).then_inc(S["c_f"], 1)
            dve.tensor_scalar(xsq[:, 0, 32:48], xsq[:, 0, 0:16], SUPPRESS, -SUPPRESS, ALU.mult, ALU.add
                              ).then_inc(S["c_scale"], 1)
            dve.wait_ge(S["c_f"], 1)
            dve.wait_ge(S["c_scale"], 1)
            dve.wait_ge(S["c_made"], 2)
            keys = ring[:, 0, 0:2 * KEYS].rearrange("p (w k) -> p w k", w=2)
            for lp in range(PAIRS):
                sel = [ring[:, 1, i * KEYS:(i + 1) * KEYS] for i in range(8)]
                if lp:
                    dve.wait_ge(S["bias_a"], 16 * lp)
                for m in range(2):
                    for s in range(2):
                        for w in range(2):
                            last = dve.tensor_scalar(sel[4 * m + 2 * s + w], keys[:, w, :],
                                                     xsq[:, 1, 4 * lp + 2 * m + s:4 * lp + 2 * m + s + 1], None,
                                                     ALU.is_equal)
                last.then_inc(S["c_eq"], 1)
                dve.wait_ge(S["c_eq"], lp + 1)
                for m in range(2):
                    dve.tensor_tensor(sel[4 * m], sel[4 * m], sel[4 * m + 1], ALU.max)
                    last = dve.tensor_tensor(sel[4 * m + 2], sel[4 * m + 2], sel[4 * m + 3], ALU.max)
                last.then_inc(S["c_m1"], 1)
                dve.wait_ge(S["c_m1"], lp + 1)
                for m in range(2):
                    last = dve.tensor_tensor(sel[4 * m + 1], sel[4 * m], sel[4 * m + 2], ALU.max)
                last.then_inc(S["c_m2"], 1)
                dve.wait_ge(S["c_m2"], lp + 1)
                selA, selB = sel[1], sel[5]
                dve.tensor_tensor(sel[3], selA, selB, ALU.is_gt).then_inc(S["c_sel"], 1)
                if lp:
                    dve.wait_ge(S["aux_st"], 16 * lp)
                for t in range(TT * NBLK):
                    dve.tensor_scalar(bias[:, t, :], selB, xsq[:, 0, 40 + t:41 + t], None, ALU.mult
                                      ).then_inc(S["bias_a"], 1)
                dve.wait_ge(S["bias_a"], 8 * (2 * lp + 1))
                dve.wait_ge(S["c_sel"], lp + 1)
                for t in range(TT * NBLK):
                    dve.scalar_tensor_tensor(out=bias[:, t, :], in0=sel[3], scalar=xsq[:, 0, 32 + t:33 + t],
                                             in1=bias[:, t, :], op0=ALU.mult, op1=ALU.add).then_inc(S["bias_a"], 1)
                dve.tensor_copy(bout, xsq[:, 0, 24 + 4 * lp:28 + 4 * lp]).then_inc(S["aux_ok"], 1)

            dve.wait_ge(S["zero"], 2)

            def kv_stage(g, j, first):
                dve.wait_ge(S["kvp"], 4 * g + j + 1)
                if not first:
                    dve.wait_ge(kv_st[j], 16 * g)
                for r in range(2):
                    rows = slice(64 * r, 64 * r + 64)
                    last = dve.tensor_copy(stM[rows, j, :, 64 * r:64 * r + 64],
                                           OB[j][rows, 0:256].rearrange("p (b k) -> p b k", k=KEYS))
                last.then_inc(S["kv_evac"], 1)

            for j in range(4):
                kv_stage(0, j, True)
            with dve.Fori(1, 8) as g:
                for j in range(4):
                    kv_stage(g, j, False)

            for lp in range(PAIRS):
                for n in range(8):
                    i = 8 * lp + n
                    dve.wait_ge(S["g_hi"], i + 1)
                    for (dst, src), (hi, _) in zip(diagonals(n, OB[i % 4], 1), diagonals(n, OB[i % 4], 0)):
                        last = lo_part(dst, src, hi)
                    last.then_inc(S["g_stage"], 1)
            def pt_lo(k, t):
                dve.wait_ge(S["pt_hi"], 8 * (k - 1) + t + 1)
                lo_part(pT[:, t % 2, 1, :], TB[:, :], pT[:, t % 2, 0, :]).then_inc(S["pt_lo"], 1)

            def ot_lo(a, j):
                dve.wait_ge(S["ot_hi"], 4 * a + j + 1)
                lo_part(oT[:, 1, j % 2, :], MX[:, :], oT[:, 0, j % 2, :]).then_inc(S["ot_lo"], 1)

            def evac(it, ph, u, first):
                k = 4 * it + ph
                own = prob[ph % 2][:, u % 4, (u // 4) * HALF:(u // 4 + 1) * HALF].rearrange("p (h k) -> p h k", k=KEYS)
                bank = SB[u % 2][:, :].rearrange("p (h k) -> p h k", k=KEYS)
                if ph < 2:
                    dve.wait_ge(S["copied"], 16 * it + 8 * ph + u + 1)
                    if not (first and ph == 0 and u < 2):
                        dve.wait_ge(S["evac"], 8 * k + u - 1)
                    dve.reduce_max(hmax[u % 2], own, AX_X).then_inc(S["maxed"], 1)
                    return
                dve.wait_ge(S["scores"], 8 * k + u + 1)
                if ph == 2 and u == 0:
                    dve.wait_ge(S["ld_aux"], 16 * (it + 1))
                row = bias[:, (ph - 2) * TT + u % 4, :].unsqueeze(1).broadcast_to([P, HH, KEYS])
                dve.scalar_tensor_tensor(out=own, in0=bank, scalar=M_SCALE, in1=row, op0=ALU.mult, op1=ALU.add
                                         ).then_inc(S["biased"], 1)
                dve.wait_ge(S["biased"], 16 * it + 8 * (ph - 2) + u + 1)
                dve.wait_ge(S["evac"], 8 * k + u - 1)
                dve.reduce_max(hmax[u % 2], own, AX_X).then_inc(S["maxed"], 1)
                dve.wait_ge(S["maxed"], 8 * k + u + 1)
                dve.tensor_tensor(own, own, hmax[u % 2].unsqueeze(2).broadcast_to([P, HH, KEYS]), ALU.subtract
                                  ).then_inc(S["evac"], 1)

            def sums(k, ph, u, first):
                dve.wait_ge(S["exped"], 8 * k + u + 1)
                own = prob[ph % 2][:, u % 4, (u // 4) * HALF:(u // 4 + 1) * HALF].rearrange("p (h k) -> p h k", k=KEYS)
                if not (first and ph == 0 and u < 2):
                    dve.wait_ge(S["summed"], 8 * k + u - 1)
                dve.reduce_sum(hsum[u % 2], own, AX_X).then_inc(S["hsummed"], 1)
                dve.wait_ge(S["hsummed"], 8 * k + u + 1)
                if not (first and ph == 0 and u < 2):
                    dve.wait_ge(S["normed"], 8 * k + u - 1)
                dve.reciprocal(rsum[u % 2], hsum[u % 2]).then_inc(S["summed"], 1)

            def xnew(it, ph, c):
                k = 4 * it + ph
                blk = (ph - 1) % 2
                dve.wait_ge(S["outd"], 4 * (k - 1) + c + 1)
                if ph in (1, 2):
                    if c == 0:
                        dve.wait_ge(S[f"ld_x{blk}"], 16 * (it + 1))
                    dve.tensor_tensor(X[blk][:, c, :], OB[c][:, :], X[blk][:, c, :], ALU.add).then_inc(S["xnew"], 1)
                else:
                    dve.scalar_tensor_tensor(out=X[blk][:, c, :], in0=OB[c][:, :], scalar=bout[:, c:c + 1],
                                             in1=X[blk][:, c, :], op0=ALU.add, op1=ALU.add).then_inc(S["xnew"], 1)

            def body(it, first):
                for ph in range(4):
                    k = 4 * it + ph
                    if ph < 2:
                        a = 2 * it + ph
                        for j in range(4):
                            dve.wait_ge(S["q_hi"], 4 * a + j + 1)
                            lo_part(qT[:, 1, j, :], PB[j][:, :], qT[:, 0, j, :]).then_inc(S["q_lo"], 1)
                            if j == 1:
                                dve.wait_ge(S["qchunk"], 4 * a + 4)
                                dve.tensor_scalar(inv[ph], OB[3][:, 0:TT], 1.0 / D, EPS, ALU.mult, ALU.add
                                                  ).then_inc(S["rmsd"], 1)
                    else:
                        for t in range(KC):
                            dve.wait_ge(S["fold_hi"], 16 * it + 8 * (ph - 2) + t + 1)
                            (src, hi), (_, lo) = fold_part(ph, t, 0), fold_part(ph, t, 1)
                            lo_part(lo, src, hi).then_inc(S["fold_lo"], 1)
                    out_of = not (first and ph == 0)
                    grouped = ph in (1, 2)
                    for u in range(STEPS):
                        if out_of:
                            pt_lo(k, u)
                        if grouped and u >= 2 and u % 2 == 0:
                            ot_lo(2 * it + ph - 1, u // 2 - 1)
                        if grouped and u == STEPS - 1:
                            ot_lo(2 * it + ph - 1, 3)
                        evac(it, ph, u, first)
                        if u > 0:
                            sums(k, ph, u - 1, first)
                    sums(k, ph, STEPS - 1, first)
                    if out_of:
                        for c in range(DC):
                            xnew(it, ph, c)

            body(0, True)
            with dve.Fori(1, ITS) as it:
                body(it, False)
            for t in range(KC):
                pt_lo(4 * ITS, t)
            for c in range(DC):
                xnew(ITS, 0, c)

        @block.gpsimd
        def _(pool):
            pool.iota(ring[:, 0, 0:KEYS], [[1, KEYS]], base=0, channel_multiplier=0,
                      allow_small_or_imprecise_dtypes=True).then_inc(S["c_made"], 1)
            pool.iota(ring[:, 0, KEYS:2 * KEYS], [[1, KEYS]], base=-KEYS, channel_multiplier=0,
                      allow_small_or_imprecise_dtypes=True).then_inc(S["c_made"], 1)
            pool.memset(ident[:, :], 0.0).then_inc(S["powd"], 1)
            pool.wait_ge(S["powd"], 1)
            pool.affine_select(out=ident[:, :], in_=ident[:, :], compare_op=ALU.not_equal, fill=1.0, base=0,
                               pattern=[[-1, P]], channel_multiplier=1).then_inc(S["idented"], 1)
            pool.wait_ge(S["c_in"], 5 * 16)
            for n in range(4):
                if n:
                    pool.wait_ge(S["wsp"], n)
                pool.dma_start(X[1][:, :, :], (wqG if n % 2 == 0 else woG)[n // 2]).then_inc(S["wsp_in"], 16)
                pool.wait_ge(S["wsp_in"], 16 * (n + 1))
                if n % 2 == 0:
                    for c in range(DC):
                        col = 16 + 4 * (n // 2) + c
                        last = pool.tensor_tensor(X[1][:, c, :], X[1][:, c, :],
                                                  xsq[:, 0, col:col + 1].broadcast_to([P, BLK]), ALU.mult)
                    last.then_inc(S["wsp_scaled"], 1)
                    pool.wait_ge(S["wsp_scaled"], n // 2 + 1)
                if n >= 2:
                    pool.wait_ge(wsp_st[n % 2], 16)
                pool.tensor_copy(stW[n % 2][:, 0], X[1][:, :, :]).then_inc(S["wsp_hi"], 1)
                pool.wait_ge(S["wsp_hi"], n + 1)
                pool.tensor_tensor(stW[n % 2][:, 1], X[1][:, :, :], stW[n % 2][:, 0].bitcast(F32), ALU.subtract
                                   ).then_inc(S["wsp"], 1)
                pool.wait_ge(S["wsp"], n + 1)
                pool.dma_start(sWG[n // 2, n % 2], stW[n % 2].bitcast(F32).rearrange("p s c n -> p s (c n)")
                               ).then_inc(wsp_st[n % 2], 16)
            pool.wait_ge(S["ctx_in"], 16)
            for i in range(8 * PAIRS):
                n = i % 8
                if n == 0:
                    pool.wait_ge(wg_in[0], 16 * (i // 8 + 1))
                if i >= 2:
                    pool.wait_ge(S["g_done"], i - 1)
                if n < 4:
                    src, times, width = wG[:, 0, :, n * HD_G:(n + 1) * HD_G], 4, HD_G
                else:
                    src, times, width = cx[:, :, (n - 4) * KEYS:(n - 3) * KEYS], 2, KEYS
                pool.tensor_copy(rep[:, i % 2].rearrange("p c (r m) -> p c r m", r=times),
                                 src.unsqueeze(2).broadcast_to([P, CC, times, width])).then_inc(S["repeated"], 1)

            pool.wait_ge(S["idented"], 4)

            def less_max(it, ph, u):
                own = prob[ph % 2][:, u % 4, (u // 4) * HALF:(u // 4 + 1) * HALF].rearrange("p (h k) -> p h k", k=KEYS)
                pool.wait_ge(S["maxed"], 8 * (4 * it + ph) + u + 1)
                pool.tensor_tensor(own, own, hmax[u % 2].unsqueeze(2).broadcast_to([P, HH, KEYS]), ALU.subtract
                                   ).then_inc(S["evac"], 1)

            def norm(it, ph, u):
                own = prob[ph % 2][:, u % 4, (u // 4) * HALF:(u // 4 + 1) * HALF].rearrange("p (h k) -> p h k", k=KEYS)
                pool.wait_ge(S["summed"], 8 * (4 * it + ph) + u + 1)
                pool.tensor_tensor(own, own, rsum[u % 2].unsqueeze(2).broadcast_to([P, HH, KEYS]), ALU.mult
                                   ).then_inc(S["normed"], 1)

            def x_lo(it, ph, c, first):
                a = 2 * it + ph
                pool.wait_ge(S["x_hi"], 4 * a + c + 1)
                if not (first and ph == 0 and c < 2):
                    pool.wait_ge(S["qchunk"], 4 * a + c - 1)
                pool.tensor_tensor(xqhl[:, 1, c % 2, :], ring[:, c, :], xqhl[:, 0, c % 2, :].bitcast(F32),
                                   ALU.subtract).then_inc(S["x_lo"], 1)
                if c == 0:
                    return
                pool.wait_ge(S["x_sq"], 4 * a + c + 1)
                if c == 1:
                    if not (first and ph == 0):
                        pool.wait_ge(S["qchunk"], 4 * a)
                    pool.tensor_tensor(sqsum[:, :], xsq[:, 0, :], xsq[:, 1, :], ALU.add).then_inc(S["sq_added"], 1)
                else:
                    pool.wait_ge(S["sq_added"], 3 * a + c - 1)
                    pool.tensor_tensor(sqsum[:, :], sqsum[:, :], xsq[:, c % 2, :], ALU.add).then_inc(S["sq_added"], 1)

            def body(it, first):
                for ph in range(4):
                    k = 4 * it + ph
                    a = 2 * it + ph
                    if ph < 2:
                        if ph == 0:
                            x_lo(it, 0, 0, first)
                            x_lo(it, 0, 1, first)
                            if not first:
                                norm(it - 1, 3, STEPS - 2)
                                norm(it - 1, 3, STEPS - 1)
                        for c in range(2, DC):
                            x_lo(it, ph, c, first)
                        pool.wait_ge(S["rmsd"], a + 1)
                        pool.tensor_tensor(inv[ph], inv[ph], mhalf, ALU.pow).then_inc(S["powd"], 1)
                        pool.wait_ge(S["powd"], a + 2)
                        pool.tensor_tensor(inv[ph], inv[ph], gscale, ALU.mult).then_inc(S["invd"], 1)
                    for u in range(STEPS):
                        if ph == 0 and u == STEPS - 1:
                            x_lo(it, 1, 0, first)
                            x_lo(it, 1, 1, first)
                        if ph < 2:
                            less_max(it, ph, u)
                            if u > 0:
                                norm(it, ph, u - 1)
                            if u == STEPS - 1:
                                norm(it, ph, u)
                        elif ph < 3 or u < STEPS - 2:
                            norm(it, ph, u)
                    if ph in (1, 2):
                        for c in range(DC):
                            pool.wait_ge(S["xb_hi"], 4 * (2 * it + ph - 1) + c + 1)
                            pool.tensor_tensor(xhl[:, 1, c, :], X[ph - 1][:, c, :], xhl[:, 0, c, :].bitcast(F32),
                                               ALU.subtract).then_inc(S["xb_lo"], 1)

            body(0, True)
            with pool.Fori(1, ITS) as it:
                body(it, False)
            norm(ITS - 1, 3, STEPS - 2)
            norm(ITS - 1, 3, STEPS - 1)


def _chunked(w):
    return w.reshape(-1, P, w.shape[1]).transpose(1, 0, 2)


def kernel(**inputs):
    import numpy as _np
    import concourse.bacc as _bacc
    from concourse import mybir as _mybir
    from concourse.bass_utils import run_bass_kernel_spmd as _run

    h = {n: _np.asarray(a) for n, a in inputs.items()}
    masked, grouped = ("L1_xattn_", "L3_xattn_"), ("L0_xattn_", "L2_xattn_")
    col_blocks = lambda w: w.reshape(CC, P, KC, P).transpose(2, 1, 0, 3)
    data = {
        "xT": h["x"].reshape(BATCH, NBLK, BLK, DC, P).transpose(0, 1, 4, 3, 2),
        "ctxT": h["ctx_2048"].reshape(BATCH * KEYS, CC, P).transpose(2, 1, 0),
        "wkvM": _np.concatenate([col_blocks(h[m + w]) for m in masked for w in ("Wk", "Wv")]),
        "wkvG": _np.stack([_np.stack([_chunked(h[g + w]) for w in ("wk", "wv")]) for g in grouped]),
        "wqG": _np.stack([_chunked(h[g + "wq"]) for g in grouped]),
        "woG": _np.stack([_chunked(h[g + "wo"]) for g in grouped]),
        "wqM": _np.stack([h[m + "Wq"].T.reshape(KC, P, D) for m in masked]),
        "woM": _np.stack([h[m + "Wo"].reshape(KC, P, D) for m in masked]),
        "normw": _np.concatenate([h[g + "norm_w"].reshape(DC, P).T for g in grouped], axis=1),
        "bo": _np.concatenate([h[m + "bo"].reshape(DC, P).T for m in masked], axis=1),
        "masks": _np.concatenate([h[m].reshape(TOKENS // P, P).T for m in ("mask_S_fk1", "mask_S_fk0")], axis=1),
        "idx": _np.stack([_np.concatenate([h[m + "token_indices_A"], h[m + "token_indices_B"]]) for m in masked]),
    }
    nc = _bacc.Bacc("TRN2", target_bir_lowering=False, num_devices=1)
    arrays, args = {}, []
    for name, a in data.items():
        a = _np.ascontiguousarray(a)
        arrays[f"in_{name}_dram"] = a
        args.append(nc.dram_tensor(f"in_{name}_dram", a.shape, _mybir.dt.from_np(a.dtype), kind="ExternalInput").ap())
    shape = (ITS + BATCH, NBLK, P, DC, BLK)
    args.append(nc.dram_tensor("out_0_dram", shape, _mybir.dt.float32, kind="ExternalOutput").ap())
    bass_cross_attention_stack(nc, *args)
    r = _run(nc, [arrays], core_ids=[0])
    xs = r.results[0]["out_0_dram"]
    return _np.ascontiguousarray(xs[ITS:].transpose(0, 1, 4, 3, 2)).reshape(BATCH, TOKENS, D)
```
